# Optimizing a Trainium2 kernel written in Bass

```python
import numpy as np
import jax
import jax.numpy as jnp

def _softmax(x, axis=-1):
    return jax.nn.softmax(x, axis=axis)

def _gelu(x):
    return jax.nn.gelu(x, approximate=True)

def _silu(x):
    return jax.nn.silu(x)

def _sigmoid(x):
    return jax.nn.sigmoid(x)

def _layernorm(x, axis=-1, eps=1e-05):
    m = jnp.mean(x, axis=axis, keepdims=True)
    v = jnp.var(x, axis=axis, keepdims=True)
    return (x - m) / jnp.sqrt(v + eps)

def _scatter_add(tgt, idx, src, axis=0):
    return tgt.at[idx].add(src)

def _segment_sum(src, seg, n):
    return jax.ops.segment_sum(src, seg, n)
kernel_name = 'mk_cond_resid_d1_seqx_r2_22f708'

def setup_inputs(seed: int=0):
    np.random.seed(seed)
    _w = jnp.asarray

    def _rec_inputs():
        import jax
        import jax.numpy as jnp
        _rk = jax.random.key(seed)
        x = -8.015e-05 + 0.9999 * jax.random.normal(jax.random.fold_in(_rk, 1), (64, 128, 1024), jnp.float32)
        _lenS = 128 - jax.random.randint(jax.random.fold_in(_rk, 7), (64,), 0, max(1, 128 // 4) + 1, jnp.int32)
        _lenS2 = 128 - jax.random.randint(jax.random.fold_in(_rk, 8), (64,), 0, max(1, 128 // 4) + 1, jnp.int32)
        cond_1024 = 0.00191187 + 0.999416 * jax.random.normal(jax.random.fold_in(_rk, 11), (64, 512), jnp.float32)
        return (x, cond_1024)
    x, cond_1024 = _rec_inputs()

    def _L0_cond_setup():
        import jax, jax.numpy as jnp
        import numpy as np
        B, N, V_DIM, Q_DIM = (128, 100, 1024, 512)
        key = jax.random.key(seed)
        k1, k2, k3, k4 = jax.random.split(key, 4)
        v = jax.random.normal(k1, (B, N, V_DIM), dtype=jnp.float32)
        q = jax.random.normal(k2, (B, Q_DIM), dtype=jnp.float32)
        W3 = jax.random.normal(k3, (Q_DIM, V_DIM), dtype=jnp.float32) * (1.0 / np.sqrt(Q_DIM))
        b3 = jnp.zeros((V_DIM,), dtype=jnp.float32)
        W2 = jax.random.normal(k4, (V_DIM, V_DIM), dtype=jnp.float32) * (1.0 / np.sqrt(V_DIM))
        b2 = jnp.zeros((V_DIM,), dtype=jnp.float32)
        return {'v': v, 'q': q, 'W3': W3, 'b3': b3, 'W2': W2, 'b2': b2}
    _L0_cond_all = _L0_cond_setup()
    _L0_cond_in = {k: v for k, v in _L0_cond_all.items() if k in ('W3', 'b3', 'W2', 'b2')}
    del _L0_cond_all
    return {'x': x, 'cond_1024': cond_1024, 'L0_cond_W3': _L0_cond_in['W3'], 'L0_cond_b3': _L0_cond_in['b3'], 'L0_cond_W2': _L0_cond_in['W2'], 'L0_cond_b2': _L0_cond_in['b2']}

def reference(x, cond_1024, L0_cond_W3, L0_cond_b3, L0_cond_W2, L0_cond_b2):
    import jax
    import jax.numpy as jnp

    def _L0_cond_ref(v, q, W3, b3, W2, b2):
        import jax, jax.numpy as jnp
        import numpy as np
        B, N, V_DIM, Q_DIM = (128, 100, 1024, 512)
        q_emb = jax.nn.relu(q @ W3 + b3)
        n = v.shape[1]
        v_sum = jnp.sum(v, axis=1, keepdims=True)
        x = (n * v + v_sum) * q_emb[:, None, :]
        return jax.nn.relu(x @ W2 + b2)
    x = x + _L0_cond_ref(x, cond_1024, L0_cond_W3, L0_cond_b3, L0_cond_W2, L0_cond_b2)
    return x

_drawn_inputs = setup_inputs


def setup_inputs(seed=0):
    import zlib

    import numpy as np

    out = dict(_drawn_inputs(seed))
    spreads = {'L0_cond_b3': (0.0, 0.1), 'L0_cond_b2': (0.0, 0.1)}
    factors = {}
    for name, (base, spread) in spreads.items():
        noise = np.random.default_rng([zlib.crc32(name.encode()), seed]).standard_normal(out[name].shape)
        drawn = base * np.exp(spread * noise) if base else spread * noise
        out[name] = jnp.asarray(drawn.astype(out[name].dtype))
    for name, factor in factors.items():
        out[name] = (out[name] * factor).astype(out[name].dtype)
    return out
```

```python
import concourse.bass as bass
from concourse import mybir
from contextlib import ExitStack


def cond_residual(nc, x_t, cond_t, w3_t, b3_t, w2, b2_t, out_t):
    fp32, fp32r = mybir.dt.float32, mybir.dt.float32r
    ALU = mybir.AluOpType
    ACT = mybir.ActivationFunctionType
    AX = mybir.AxisListType

    GROUPS, P, KT, GB, N = x_t.shape
    COLS = GB * N
    QT, B = cond_t.shape[1:]
    D = KT * P
    HALF = KT // 2
    X_SLOTS, STAGES, SCALED_SLOTS = 2, 3, 4
    LAST = KT - 1
    OUT_PAIRS = KT // 2

    ctx = ExitStack()
    with ctx:
        def sb(name, shape, dt=fp32):
            return ctx.enter_context(nc.sbuf_tensor(name, shape, dt))

        def sem(name):
            return ctx.enter_context(nc.semaphore(name))

        w_hi = sb("w_hi", [P, KT, D], fp32r)
        w_lo = sb("w_lo", [P, KT, D], fp32r)
        w2_stage = sb("w2_stage", [P, STAGES, D])
        w3_stage = sb("w3_stage", [P, STAGES, QT, P])
        cond_sb = sb("cond_sb", [P, QT, B])
        b3_sb = sb("b3_sb", [P, KT])
        b2_sb = sb("b2_sb", [P, KT])
        q_emb = sb("q_emb", [P, KT, B])
        x_sb = sb("x_sb", [P, X_SLOTS, KT, GB, N])
        x_hi = sb("x_hi", [P, 2, KT, COLS], fp32r)
        x_lo = sb("x_lo", [P, 2, KT, COLS], fp32r)
        scaled = sb("scaled", [P, SCALED_SLOTS, COLS])
        vsum = sb("vsum", [P, 2, KT, GB])
        scale = sb("scale", [P, 2, KT, GB])
        bias = sb("bias", [P, 2, KT, GB])
        out_sb = sb("out_sb", [P, 2, 2, COLS])
        acc = ctx.enter_context(nc.psum_tensor("acc", [P, KT, COLS], fp32))

        cond_loaded, bias_loaded = sem("cond_loaded"), sem("bias_loaded")
        w3_loaded = [sem(f"w3_loaded{s}") for s in range(STAGES)]
        w2_loaded = [sem(f"w2_loaded{s}") for s in range(STAGES)]
        x0_loaded = [sem(f"x0_loaded{k}") for k in range(KT)]
        x_loaded = [[sem(f"x_loaded{s}_{h}") for h in range(2)] for s in range(X_SLOTS)]
        stored = [sem(f"stored{s}") for s in range(2)]
        tail_stored = sem("tail_stored")
        q_summed, q_ready = sem("q_summed"), sem("q_ready")
        w_hi_ready, w_lo_ready = sem("w_hi_ready"), sem("w_lo_ready")
        scaled_ready, x_hi_ready, x_lo_ready = sem("scaled_ready"), sem("x_hi_ready"), sem("x_lo_ready")
        acc_done, relu_done, out_ready = sem("acc_done"), sem("relu_done"), sem("out_ready")
        vsum_ready, scalars_ready = sem("vsum_ready"), sem("scalars_ready")

        def scalar_steps(g, h):
            return KT + 2 * (g - 1) + h + 1

        block = ctx.enter_context(nc.Block())

        @block.sync
        def _(sp):
            for k in range(KT):
                if k >= STAGES:
                    sp.wait_ge(q_summed, k - STAGES + 1)
                sp.dma_start(w3_stage[:, k % STAGES], w3_t[k]).then_inc(w3_loaded[k % STAGES], 16)
                sp.dma_start(x_sb[:, 0, k], x_t[0, :, k]).then_inc(x0_loaded[k], 16)
                if k >= STAGES:
                    sp.wait_ge(w_lo_ready, k - STAGES + 1)
                sp.dma_start(w2_stage[:, k % STAGES], w2[k * P:(k + 1) * P, :]).then_inc(w2_loaded[k % STAGES], 16)
            for h in range(2):
                half = slice(h * HALF, (h + 1) * HALF)
                sp.dma_start(x_sb[:, 1, half], x_t[1, :, half]).then_inc(x_loaded[1][h], 16)

            def store(g, j):
                sp.wait_ge(out_ready, KT * g + 2 * j + 2)
                sp.dma_start(out_t[g, :, 2 * j:2 * j + 2], out_sb[:, j % 2]).then_inc(stored[j % 2], 16)

            def group(g, slot, load):
                for j in range(OUT_PAIRS):
                    store(g, j)
                    if load and j % 2:
                        half = slice(j // 2 * HALF, (j // 2 + 1) * HALF)
                        sp.dma_start(x_sb[:, slot, half], x_t[g + 2, :, half]).then_inc(x_loaded[slot][j // 2], 16)

            group(0, 0, True)
            with sp.Fori(0, (GROUPS - 4) // 2) as i:
                group(2 * i + 1, 1, True)
                group(2 * i + 2, 0, True)
            group(GROUPS - 3, 1, True)
            group(GROUPS - 2, 0, False)
            for j in range(OUT_PAIRS - 1):
                store(GROUPS - 1, j)
            j = OUT_PAIRS - 1
            for r in range(2):
                sp.wait_ge(out_ready, KT * (GROUPS - 1) + 2 * j + r + 1)
                sp.dma_start(out_t[GROUPS - 1, :, 2 * j + r], out_sb[:, j % 2, r]).then_inc(tail_stored, 16)
            sp.wait_ge(stored[0], 16 * 2 * GROUPS)
            sp.wait_ge(stored[1], 16 * (2 * GROUPS - 1))
            sp.wait_ge(tail_stored, 32)

        @block.tensor
        def _(pe):
            def product(dst, w, x, k, m, slot, start=False, stop=False):
                return nc.tensor.matmul(dst, w[:, k, m * P:(m + 1) * P], x[:, slot, k], start=start, stop=stop)

            def q_sum(k):
                pe.wait_ge(w3_loaded[k % STAGES], 16 * (k // STAGES + 1))
                if k == 0:
                    pe.wait_ge(cond_loaded, 16)
                if k >= 1:
                    pe.wait_ge(q_ready, k)
                for t in range(QT):
                    last = nc.tensor.matmul(acc[:, LAST, k * B:(k + 1) * B], w3_stage[:, k % STAGES, t],
                                            cond_sb[:, t], start=(t == 0), stop=(t == QT - 1))
                last.then_inc(q_summed, 1)

            q_sum(0)
            for k in range(KT):
                if k + 1 < KT:
                    q_sum(k + 1)
                pe.wait_ge(w_hi_ready, k + 1)
                pe.wait_ge(x_hi_ready, k + 1)
                for m in range(LAST):
                    product(acc[:, m], w_hi, x_hi, k, m, 0, start=(k == 0))
                pe.wait_ge(x_lo_ready, k + 1)
                for m in range(LAST):
                    product(acc[:, m], w_hi, x_lo, k, m, 0)
                pe.wait_ge(w_lo_ready, k + 1)
                for m in range(LAST):
                    last = product(acc[:, m], w_lo, x_hi, k, m, 0, stop=(k == KT - 1))
                    if k == KT - 1:
                        last.then_inc(acc_done, 1)
            pe.wait_ge(q_ready, KT)
            for k in range(KT):
                product(acc[:, LAST], w_hi, x_hi, k, LAST, 0, start=(k == 0))
                product(acc[:, LAST], w_hi, x_lo, k, LAST, 0)
                last = product(acc[:, LAST], w_lo, x_hi, k, LAST, 0, stop=(k == KT - 1))
            last.then_inc(acc_done, 1)

            def group(g, slot):
                for m in range(KT):
                    pe.wait_ge(relu_done, KT * (g - 1) + m + 1)
                    for k in range(KT):
                        if m == 0:
                            pe.wait_ge(x_lo_ready, KT * g + k + 1)
                        product(acc[:, m], w_hi, x_hi, k, m, slot, start=(k == 0))
                        product(acc[:, m], w_hi, x_lo, k, m, slot)
                        last = product(acc[:, m], w_lo, x_hi, k, m, slot, stop=(k == KT - 1))
                    last.then_inc(acc_done, 1)

            with pe.Fori(0, (GROUPS - 2) // 2) as i:
                group(2 * i + 1, 1)
                group(2 * i + 2, 0)
            group(GROUPS - 1, 1)

        @block.scalar
        def _(act):
            act.dma_start(cond_sb[:], cond_t).then_inc(cond_loaded, 16)
            act.dma_start(b3_sb[:], b3_t).then_inc(bias_loaded, 16)
            act.dma_start(b2_sb[:], b2_t).then_inc(bias_loaded, 16)

            def scale_x(g, k, slot, first=False):
                if not (first and k < SCALED_SLOTS):
                    act.wait_ge(x_lo_ready, KT * g + k - SCALED_SLOTS + 1)
                for b in range(GB):
                    last = nc.scalar.activation(scaled[:, k % SCALED_SLOTS, b * N:(b + 1) * N], x_sb[:, slot, k, b],
                                                ACT.Identity, bias=bias[:, slot, k, b:b + 1],
                                                scale=scale[:, slot, k, b:b + 1])
                last.then_inc(scaled_ready, 1)

            def relu(g, m, first=False):
                j = m // 2
                act.wait_ge(acc_done, KT * g + m + 1)
                if m % 2 == 0 and not (first and j < 2):
                    act.wait_ge(stored[j % 2], 16 * (2 * g + j // 2))
                nc.scalar.activation(out_sb[:, j % 2, m % 2], acc[:, m], ACT.Relu,
                                     bias=b2_sb[:, m:m + 1]).then_inc(relu_done, 1)

            act.wait_ge(bias_loaded, 32)
            for k in range(KT):
                act.wait_ge(q_summed, k + 1)
                nc.scalar.activation(q_emb[:, k], acc[:, LAST, k * B:(k + 1) * B], ACT.Relu,
                                     bias=b3_sb[:, k:k + 1]).then_inc(q_ready, 1)
                act.wait_ge(w2_loaded[k % STAGES], 16 * (k // STAGES + 1))
                nc.scalar.copy(w_hi[:, k], w2_stage[:, k % STAGES]).then_inc(w_hi_ready, 1)
                act.wait_ge(scalars_ready, k + 1)
                scale_x(0, k, 0, first=True)
            for k in range(KT):
                if k % HALF == 0:
                    act.wait_ge(scalars_ready, scalar_steps(1, k // HALF))
                scale_x(1, k, 1)
            for m in range(KT):
                relu(0, m, first=True)

            def group(g, slot):
                for m in range(KT):
                    for k in range(2 * m, min(2 * m + 2, KT)):
                        if k % HALF == 0:
                            act.wait_ge(scalars_ready, scalar_steps(g + 1, k // HALF))
                        scale_x(g + 1, k, 1 - slot)
                    relu(g, m)

            with act.Fori(0, (GROUPS - 2) // 2) as i:
                group(2 * i + 1, 1)
                group(2 * i + 2, 0)
            for m in range(KT):
                relu(GROUPS - 1, m)

        @block.vector
        def _(dve):
            def scalars(g, slot, k0, k1, step, first=False):
                if not first:
                    dve.wait_ge(scaled_ready, KT * (g - 1))
                nc.vector.tensor_reduce(vsum[:, slot, k0:k1], x_sb[:, slot, k0:k1], AX.X,
                                        ALU.add).then_inc(vsum_ready, 1)
                if first:
                    dve.wait_ge(q_ready, k1)
                q = q_emb[:, k0:k1, bass.ds(GB * g, GB)]
                nc.vector.tensor_scalar(scale[:, slot, k0:k1], q, float(N), None, ALU.mult)
                dve.wait_ge(vsum_ready, step)
                nc.vector.tensor_tensor(bias[:, slot, k0:k1], vsum[:, slot, k0:k1], q,
                                        ALU.mult).then_inc(scalars_ready, 1)

            def split_hi(g, k, slot):
                dve.wait_ge(scaled_ready, KT * g + k + 1)
                nc.vector.tensor_copy(x_hi[:, slot, k], scaled[:, k % SCALED_SLOTS]).then_inc(x_hi_ready, 1)

            def split_lo(g, k, slot):
                dve.wait_ge(x_hi_ready, KT * g + k + 1)
                nc.vector.tensor_tensor(x_lo[:, slot, k], scaled[:, k % SCALED_SLOTS],
                                        x_hi[:, slot, k].bitcast(fp32), ALU.subtract).then_inc(x_lo_ready, 1)

            def add_x(g, m, slot):
                dve.wait_ge(relu_done, KT * g + m + 1)
                o = out_sb[:, m // 2 % 2, m % 2]
                nc.vector.tensor_tensor(o, o, x_sb[:, slot, m].rearrange("p b n -> p (b n)"),
                                        ALU.add).then_inc(out_ready, 1)

            for k in range(KT):
                dve.wait_ge(x0_loaded[k], 16)
                scalars(0, 0, k, k + 1, k + 1, first=True)
                split_hi(0, k, 0)
                split_lo(0, k, 0)
                dve.wait_ge(w_hi_ready, k + 1)
                nc.vector.tensor_tensor(w_lo[:, k], w2_stage[:, k % STAGES], w_hi[:, k].bitcast(fp32),
                                        ALU.subtract).then_inc(w_lo_ready, 1)
            for k in range(KT):
                h = k // HALF
                if k % HALF == 0:
                    dve.wait_ge(x_loaded[1][h], 16)
                    scalars(1, 1, k, k + HALF, scalar_steps(1, h), first=True)
                split_hi(1, k, 1)
                split_lo(1, k, 1)
            for m in range(KT):
                add_x(0, m, 0)

            def group(g, slot, loads):
                for m in range(KT):
                    for k in range(2 * m, min(2 * m + 2, KT)):
                        h = k // HALF
                        if k % HALF == 0:
                            dve.wait_ge(x_loaded[1 - slot][h], 16 * loads)
                            scalars(g + 1, 1 - slot, k, k + HALF, scalar_steps(g + 1, h))
                        if k == 0:
                            dve.wait_ge(acc_done, KT * g)
                        split_hi(g + 1, k, 1 - slot)
                        split_lo(g + 1, k, 1 - slot)
                    add_x(g, m, slot)

            with dve.Fori(0, (GROUPS - 2) // 2) as i:
                group(2 * i + 1, 1, i + 1)
                group(2 * i + 2, 0, i + 2)
            for m in range(KT):
                add_x(GROUPS - 1, m, 1)


def kernel(x, cond_1024, L0_cond_W3, L0_cond_b3, L0_cond_W2, L0_cond_b2):
    import numpy as np
    import concourse.bacc as bacc
    from concourse.bass_utils import run_bass_kernel_spmd

    P, GB = 128, 4
    x = np.asarray(x)
    B, N, D = x.shape
    KT, Q = D // P, cond_1024.shape[1]
    G, QT = B // GB, Q // P
    arrays = {
        "x_t": x.reshape(G, GB, N, KT, P).transpose(0, 4, 3, 1, 2),
        "cond_t": np.asarray(cond_1024).reshape(B, QT, P).transpose(2, 1, 0),
        "w3_t": np.asarray(L0_cond_W3).reshape(QT, P, KT, P).transpose(2, 1, 0, 3),
        "b3_t": np.asarray(L0_cond_b3).reshape(KT, P).T,
        "w2": np.asarray(L0_cond_W2),
        "b2_t": np.asarray(L0_cond_b2).reshape(KT, P).T,
    }
    arrays = {name: np.ascontiguousarray(a) for name, a in arrays.items()}
    nc = bacc.Bacc("TRN2", target_bir_lowering=False, num_devices=1)
    args = [nc.dram_tensor(name, a.shape, mybir.dt.from_np(a.dtype), kind="ExternalInput").ap()
            for name, a in arrays.items()]
    out = nc.dram_tensor("out_t", (G, P, KT, GB, N), mybir.dt.float32, kind="ExternalOutput").ap()
    cond_residual(nc, *args, out)
    r = run_bass_kernel_spmd(nc, [arrays], core_ids=[0])
    return r.results[0]["out_t"].transpose(0, 3, 4, 2, 1).reshape(B, N, D)
```

```python
import concourse.bass as bass
from concourse import mybir
from contextlib import ExitStack


def cond_residual(nc, x_t, small_t, w3_t, w2, out_t):
    fp32, fp32r = mybir.dt.float32, mybir.dt.float32r
    ALU = mybir.AluOpType
    ACT = mybir.ActivationFunctionType
    AX = mybir.AxisListType

    GROUPS, P, KT, GB, N = x_t.shape
    COLS = GB * N
    QT, B = w3_t.shape[2], GROUPS * GB
    D = KT * P
    HALF = KT // 2
    X_SLOTS, W3_STAGES, STAGES, SCALED_SLOTS = 2, 4, 3, 4
    LAST = KT - 1
    WARM_UP, WARM_GAP = 7, 4
    OUT_PAIRS = KT // 2

    ctx = ExitStack()
    with ctx:
        def sb(name, shape, dt=fp32):
            return ctx.enter_context(nc.sbuf_tensor(name, shape, dt))

        def sem(name):
            return ctx.enter_context(nc.semaphore(name))

        w_hi = sb("w_hi", [P, KT, D], fp32r)
        w_lo = sb("w_lo", [P, KT, D], fp32r)
        w2_stage = sb("w2_stage", [P, STAGES, D])
        w3_stage = sb("w3_stage", [P, W3_STAGES, QT, P])
        small_sb = sb("small_sb", [P, QT * B + 2 * KT])
        cond_sb = small_sb[:, :QT * B].rearrange("p (t b) -> p t b", t=QT)
        b3_sb = small_sb[:, QT * B:QT * B + KT]
        b2_sb = small_sb[:, QT * B + KT:]
        q_emb = sb("q_emb", [P, KT, B])
        x_sb = sb("x_sb", [P, X_SLOTS, KT, GB, N])
        x_hi = sb("x_hi", [P, 2, KT, COLS], fp32r)
        x_lo = sb("x_lo", [P, 2, KT, COLS], fp32r)
        scaled = sb("scaled", [P, SCALED_SLOTS, COLS])
        vsum = sb("vsum", [P, 2, KT, GB])
        scale = sb("scale", [P, 2, KT, GB])
        bias = sb("bias", [P, 2, KT, GB])
        out_sb = sb("out_sb", [P, 2, 2, COLS])
        acc = ctx.enter_context(nc.psum_tensor("acc", [P, KT, COLS], fp32))

        table_scratch = sb("table_scratch", [P, 1])
        warm = sb("warm", [P, COLS], mybir.dt.bfloat16)
        table_set, warm_set = sem("table_set"), sem("warm_set")

        small_loaded = sem("small_loaded")
        w3_loaded = [sem(f"w3_loaded{s}") for s in range(W3_STAGES)]
        w2_loaded = [sem(f"w2_loaded{s}") for s in range(STAGES)]
        x0_loaded = [sem(f"x0_loaded{k}") for k in range(KT)]
        x_loaded = [[sem(f"x_loaded{s}_{h}") for h in range(2)] for s in range(X_SLOTS)]
        stored = [sem(f"stored{s}") for s in range(2)]
        tail_stored = sem("tail_stored")
        q_summed, q_ready = sem("q_summed"), sem("q_ready")
        w_hi_ready, w_lo_ready = sem("w_hi_ready"), sem("w_lo_ready")
        scaled_ready, x_hi_ready, x_lo_ready = sem("scaled_ready"), sem("x_hi_ready"), sem("x_lo_ready")
        acc_done, relu_done, out_ready = sem("acc_done"), sem("relu_done"), sem("out_ready")
        vsum_ready, scalars_ready = sem("vsum_ready"), sem("scalars_ready")

        def scalar_steps(g, h):
            return KT + 2 * (g - 1) + h + 1

        block = ctx.enter_context(nc.Block())

        @block.sync
        def _(sp):
            for k in range(KT):
                if k >= W3_STAGES:
                    sp.wait_ge(q_summed, k - W3_STAGES + 1)
                sp.dma_start(w3_stage[:, k % W3_STAGES], w3_t[k]).then_inc(w3_loaded[k % W3_STAGES], 16)
                sp.dma_start(x_sb[:, 0, k], x_t[0, :, k]).then_inc(x0_loaded[k], 16)
                if k >= STAGES:
                    sp.wait_ge(w_lo_ready, k - STAGES + 1)
                sp.dma_start(w2_stage[:, k % STAGES], w2[k * P:(k + 1) * P, :]).then_inc(w2_loaded[k % STAGES], 16)
            for h in range(2):
                half = slice(h * HALF, (h + 1) * HALF)
                sp.dma_start(x_sb[:, 1, half], x_t[1, :, half]).then_inc(x_loaded[1][h], 16)

            def store(g, j):
                sp.wait_ge(out_ready, KT * g + 2 * j + 2)
                sp.dma_start(out_t[g, :, 2 * j:2 * j + 2], out_sb[:, j % 2]).then_inc(stored[j % 2], 16)

            def group(g, slot, load):
                for j in range(OUT_PAIRS):
                    store(g, j)
                    if load and j % 2:
                        half = slice(j // 2 * HALF, (j // 2 + 1) * HALF)
                        sp.dma_start(x_sb[:, slot, half], x_t[g + 2, :, half]).then_inc(x_loaded[slot][j // 2], 16)

            group(0, 0, True)
            with sp.Fori(0, (GROUPS - 4) // 2) as i:
                group(2 * i + 1, 1, True)
                group(2 * i + 2, 0, True)
            group(GROUPS - 3, 1, True)
            group(GROUPS - 2, 0, False)
            for j in range(OUT_PAIRS - 1):
                store(GROUPS - 1, j)
            j = OUT_PAIRS - 1
            for r in range(2):
                sp.wait_ge(out_ready, KT * (GROUPS - 1) + 2 * j + r + 1)
                sp.dma_start(out_t[GROUPS - 1, :, 2 * j + r], out_sb[:, j % 2, r]).then_inc(tail_stored, 16)
            sp.wait_ge(stored[0], 16 * 2 * GROUPS)
            sp.wait_ge(stored[1], 16 * (2 * GROUPS - 1))
            sp.wait_ge(tail_stored, 32)

        @block.tensor
        def _(pe):
            def product(dst, w, x, k, m, slot, start=False, stop=False):
                return nc.tensor.matmul(dst, w[:, k, m * P:(m + 1) * P], x[:, slot, k], start=start, stop=stop)

            def q_sum(k):
                pe.wait_ge(w3_loaded[k % W3_STAGES], 16 * (k // W3_STAGES + 1))
                if k == 0:
                    pe.wait_ge(small_loaded, 16)
                if k >= 1:
                    pe.wait_ge(q_ready, k)
                for t in range(QT):
                    last = nc.tensor.matmul(acc[:, LAST, k * B:(k + 1) * B], w3_stage[:, k % W3_STAGES, t],
                                            cond_sb[:, t], start=(t == 0), stop=(t == QT - 1))
                last.then_inc(q_summed, 1)

            def keep_warm(n):
                for _ in range(n):
                    nc.tensor.matmul(acc[:, 0], warm[:, :P], warm[:], start=True, stop=True)

            pe.wait_ge(warm_set, 1)
            keep_warm(WARM_UP)
            q_sum(0)
            keep_warm(WARM_GAP)
            q_sum(1)
            for k in range(KT):
                pe.wait_ge(w_hi_ready, k + 1)
                pe.wait_ge(x_hi_ready, k + 1)
                for m in range(LAST):
                    product(acc[:, m], w_hi, x_hi, k, m, 0, start=(k == 0))
                if k == 0:
                    q_sum(2)
                pe.wait_ge(x_lo_ready, k + 1)
                for m in range(LAST):
                    product(acc[:, m], w_hi, x_lo, k, m, 0)
                if k + 3 < KT:
                    q_sum(k + 3)
                pe.wait_ge(w_lo_ready, k + 1)
                for m in range(LAST):
                    last = product(acc[:, m], w_lo, x_hi, k, m, 0, stop=(k == KT - 1))
                    if k == KT - 1:
                        last.then_inc(acc_done, 1)
            pe.wait_ge(q_ready, KT)
            for k in range(KT):
                product(acc[:, LAST], w_hi, x_hi, k, LAST, 0, start=(k == 0))
                product(acc[:, LAST], w_hi, x_lo, k, LAST, 0)
                last = product(acc[:, LAST], w_lo, x_hi, k, LAST, 0, stop=(k == KT - 1))
            last.then_inc(acc_done, 1)

            def group(g, slot):
                for m in range(KT):
                    pe.wait_ge(relu_done, KT * (g - 1) + m + 1)
                    for k in range(KT):
                        if m == 0:
                            pe.wait_ge(x_lo_ready, KT * g + k + 1)
                        product(acc[:, m], w_hi, x_hi, k, m, slot, start=(k == 0))
                        product(acc[:, m], w_hi, x_lo, k, m, slot)
                        last = product(acc[:, m], w_lo, x_hi, k, m, slot, stop=(k == KT - 1))
                    last.then_inc(acc_done, 1)

            with nc.Fori(0, (GROUPS - 2) // 2, engines=(mybir.EngineType.PE,), hint_back_edge=True) as i:
                group(2 * i + 1, 1)
                group(2 * i + 2, 0)
            group(GROUPS - 1, 1)

        @block.scalar
        def _(act):
            act.dma_start(small_sb[:], small_t).then_inc(small_loaded, 16)

            def scale_x(g, k, slot, first=False):
                if not (first and k < SCALED_SLOTS):
                    act.wait_ge(x_lo_ready, KT * g + k - SCALED_SLOTS + 1)
                for b in range(GB):
                    last = nc.scalar.activation(scaled[:, k % SCALED_SLOTS, b * N:(b + 1) * N], x_sb[:, slot, k, b],
                                                ACT.Identity, bias=bias[:, slot, k, b:b + 1],
                                                scale=scale[:, slot, k, b:b + 1])
                last.then_inc(scaled_ready, 1)

            def relu(g, m, first=False):
                j = m // 2
                act.wait_ge(acc_done, KT * g + m + 1)
                if m % 2 == 0 and not (first and j < 2):
                    act.wait_ge(stored[j % 2], 16 * (2 * g + j // 2))
                nc.scalar.activation(out_sb[:, j % 2, m % 2], acc[:, m], ACT.Relu,
                                     bias=b2_sb[:, m:m + 1]).then_inc(relu_done, 1)

            def q_relu(k):
                act.wait_ge(q_summed, k + 1)
                nc.scalar.activation(q_emb[:, k], acc[:, LAST, k * B:(k + 1) * B], ACT.Relu,
                                     bias=b3_sb[:, k:k + 1]).then_inc(q_ready, 1)

            act.wait_ge(table_set, 1)
            nc.scalar.activation(table_scratch[:], table_scratch[:], ACT.Relu)
            act.wait_ge(small_loaded, 16)
            q_relu(0)
            for k in range(KT):
                if 1 <= k < KT - 1:
                    q_relu(k + 1)
                if k >= 1:
                    act.wait_ge(scalars_ready, k + 1)
                    scale_x(0, k, 0, first=True)
                act.wait_ge(w2_loaded[k % STAGES], 16 * (k // STAGES + 1))
                nc.scalar.copy(w_hi[:, k], w2_stage[:, k % STAGES]).then_inc(w_hi_ready, 1)
                if k == 0:
                    q_relu(1)
            for k in range(KT):
                if k % HALF == 0:
                    act.wait_ge(scalars_ready, scalar_steps(1, k // HALF))
                scale_x(1, k, 1)
                if k >= KT - 2:
                    relu(0, k - (KT - 2), first=True)
            for m in range(2, KT):
                relu(0, m, first=True)

            def group(g, slot):
                for m in range(KT):
                    for k in range(2 * m, min(2 * m + 2, KT)):
                        if k % HALF == 0:
                            act.wait_ge(scalars_ready, scalar_steps(g + 1, k // HALF))
                        scale_x(g + 1, k, 1 - slot)
                    relu(g, m)

            with act.Fori(0, (GROUPS - 2) // 2) as i:
                group(2 * i + 1, 1)
                group(2 * i + 2, 0)
            for m in range(KT):
                relu(GROUPS - 1, m)

        @block.vector
        def _(dve):
            def scalars(g, slot, k0, k1, step, first=False):
                if not first:
                    dve.wait_ge(scaled_ready, KT * (g - 1))
                nc.vector.tensor_reduce(vsum[:, slot, k0:k1], x_sb[:, slot, k0:k1], AX.X,
                                        ALU.add).then_inc(vsum_ready, 1)
                if first:
                    dve.wait_ge(q_ready, k1)
                q = q_emb[:, k0:k1, bass.ds(GB * g, GB)]
                nc.vector.tensor_scalar(scale[:, slot, k0:k1], q, float(N), None, ALU.mult)
                dve.wait_ge(vsum_ready, step)
                nc.vector.tensor_tensor(bias[:, slot, k0:k1], vsum[:, slot, k0:k1], q,
                                        ALU.mult).then_inc(scalars_ready, 1)

            def split_hi(g, k, slot):
                dve.wait_ge(scaled_ready, KT * g + k + 1)
                nc.vector.tensor_copy(x_hi[:, slot, k], scaled[:, k % SCALED_SLOTS]).then_inc(x_hi_ready, 1)

            def split_lo(g, k, slot):
                dve.wait_ge(x_hi_ready, KT * g + k + 1)
                nc.vector.tensor_tensor(x_lo[:, slot, k], scaled[:, k % SCALED_SLOTS],
                                        x_hi[:, slot, k].bitcast(fp32), ALU.subtract).then_inc(x_lo_ready, 1)

            def add_x(g, m, slot):
                dve.wait_ge(relu_done, KT * g + m + 1)
                o = out_sb[:, m // 2 % 2, m % 2]
                nc.vector.tensor_tensor(o, o, x_sb[:, slot, m].rearrange("p b n -> p (b n)"),
                                        ALU.add).then_inc(out_ready, 1)

            def scalars_0(k):
                dve.wait_ge(x0_loaded[k], 16)
                scalars(0, 0, k, k + 1, k + 1, first=True)

            def scalars_1(h):
                dve.wait_ge(x_loaded[1][h], 16)
                scalars(1, 1, h * HALF, (h + 1) * HALF, scalar_steps(1, h), first=True)

            nc.vector.memset(warm[:], 0.0).then_inc(warm_set, 1)
            nc.vector.memset(table_scratch[:], 0.0).then_inc(table_set, 1)
            scalars_0(0)
            dve.wait_ge(scalars_ready, 1)
            for b in range(GB):
                last = nc.vector.tensor_scalar(scaled[:, 0, b * N:(b + 1) * N], x_sb[:, 0, 0, b],
                                               scale[:, 0, 0, b:b + 1], bias[:, 0, 0, b:b + 1], ALU.mult, ALU.add)
            last.then_inc(scaled_ready, 1)
            for k in range(KT):
                if 1 <= k < KT - 1:
                    scalars_0(k + 1)
                if k == KT - 1:
                    scalars_1(0)
                split_hi(0, k, 0)
                split_lo(0, k, 0)
                dve.wait_ge(w_hi_ready, k + 1)
                nc.vector.tensor_tensor(w_lo[:, k], w2_stage[:, k % STAGES], w_hi[:, k].bitcast(fp32),
                                        ALU.subtract).then_inc(w_lo_ready, 1)
                if k == 0:
                    scalars_0(1)
            for k in range(KT):
                if k == 1:
                    scalars_1(1)
                split_hi(1, k, 1)
                split_lo(1, k, 1)
            for m in range(KT):
                add_x(0, m, 0)

            def group(g, slot, loads):
                for m in range(KT):
                    for k in range(2 * m, min(2 * m + 2, KT)):
                        h = k // HALF
                        if k % HALF == 0:
                            dve.wait_ge(x_loaded[1 - slot][h], 16 * loads)
                            scalars(g + 1, 1 - slot, k, k + HALF, scalar_steps(g + 1, h))
                        if k == 0:
                            dve.wait_ge(acc_done, KT * g)
                        split_hi(g + 1, k, 1 - slot)
                        split_lo(g + 1, k, 1 - slot)
                    add_x(g, m, slot)

            with dve.Fori(0, (GROUPS - 2) // 2) as i:
                group(2 * i + 1, 1, i + 1)
                group(2 * i + 2, 0, i + 2)
            for m in range(KT):
                add_x(GROUPS - 1, m, 1)


def kernel(x, cond_1024, L0_cond_W3, L0_cond_b3, L0_cond_W2, L0_cond_b2):
    import numpy as np
    import concourse.bacc as bacc
    from concourse.bass_utils import run_bass_kernel_spmd

    P, GB = 128, 4
    x = np.asarray(x)
    B, N, D = x.shape
    KT, Q = D // P, cond_1024.shape[1]
    G, QT = B // GB, Q // P
    arrays = {
        "x_t": x.reshape(G, GB, N, KT, P).transpose(0, 4, 3, 1, 2),
        "small_t": np.concatenate([np.asarray(cond_1024).reshape(B, QT, P).transpose(2, 1, 0).reshape(P, QT * B),
                                   np.asarray(L0_cond_b3).reshape(KT, P).T,
                                   np.asarray(L0_cond_b2).reshape(KT, P).T], axis=1),
        "w3_t": np.asarray(L0_cond_W3).reshape(QT, P, KT, P).transpose(2, 1, 0, 3),
        "w2": np.asarray(L0_cond_W2),
    }
    arrays = {name: np.ascontiguousarray(a) for name, a in arrays.items()}
    nc = bacc.Bacc("TRN2", target_bir_lowering=False, num_devices=1)
    args = [nc.dram_tensor(name, a.shape, mybir.dt.from_np(a.dtype), kind="ExternalInput").ap()
            for name, a in arrays.items()]
    out = nc.dram_tensor("out_t", (G, P, KT, GB, N), mybir.dt.float32, kind="ExternalOutput").ap()
    cond_residual(nc, *args, out)
    r = run_bass_kernel_spmd(nc, [arrays], core_ids=[0])
    return r.results[0]["out_t"].transpose(0, 3, 4, 2, 1).reshape(B, N, D)
```
